# Optimizing a Trainium2 kernel written in Bass

```python
import numpy as np
import jax
import jax.numpy as jnp

def _softmax(x, axis=-1):
    return jax.nn.softmax(x, axis=axis)

def _gelu(x):
    return jax.nn.gelu(x, approximate=True)

def _silu(x):
    return jax.nn.silu(x)

def _sigmoid(x):
    return jax.nn.sigmoid(x)

def _layernorm(x, axis=-1, eps=1e-05):
    m = jnp.mean(x, axis=axis, keepdims=True)
    v = jnp.var(x, axis=axis, keepdims=True)
    return (x - m) / jnp.sqrt(v + eps)

def _scatter_add(tgt, idx, src, axis=0):
    return tgt.at[idx].add(src)

def _segment_sum(src, seg, n):
    return jax.ops.segment_sum(src, seg, n)
kernel_name = 'mk_cond_resid_d1_seqx_r2_4b7b71'

def setup_inputs(seed: int=0):
    np.random.seed(seed)
    _w = jnp.asarray

    def _rec_inputs():
        import jax
        import jax.numpy as jnp
        _rk = jax.random.key(seed)
        x = -0.000125 + 0.9999 * jax.random.normal(jax.random.fold_in(_rk, 1), (16, 512, 512), jnp.float32)
        _lenS = 512 - jax.random.randint(jax.random.fold_in(_rk, 7), (16,), 0, max(1, 512 // 4) + 1, jnp.int32)
        _lenS2 = 512 - jax.random.randint(jax.random.fold_in(_rk, 8), (16,), 0, max(1, 512 // 4) + 1, jnp.int32)
        itok_B_0_7 = jax.random.randint(jax.random.fold_in(_rk, 11), (16,), 0, 8, jnp.int32)
        return (x, itok_B_0_7)
    x, itok_B_0_7 = _rec_inputs()

    def _L0_cond_setup():
        import jax, jax.numpy as jnp
        import numpy as np
        IN, HID, OUT, PART, E = (512, 2048, 512, 128, 8)
        B, N = (16, 1024)
        key = jax.random.key(seed)
        ks = jax.random.split(key, 8)
        s1 = 1.0 / np.sqrt(IN)
        s2 = 1.0 / np.sqrt(HID)
        return {'x': jax.random.normal(ks[0], (B, N, IN), dtype=jnp.float32), 'indices': jax.random.randint(ks[1], (B,), 0, E, dtype=jnp.int64), 'W1': jax.random.uniform(ks[2], (IN, HID), jnp.float32, -s1, s1), 'b1': jax.random.uniform(ks[3], (HID,), jnp.float32, -s1, s1), 'W2': jax.random.uniform(ks[4], (HID, OUT - PART), jnp.float32, -s2, s2), 'b2': jax.random.uniform(ks[5], (OUT - PART,), jnp.float32, -s2, s2), 'We': jax.random.uniform(ks[6], (E, HID, PART), jnp.float32, -s2, s2), 'be': jax.random.uniform(ks[7], (E, PART), jnp.float32, -s2, s2)}
    _L0_cond_all = _L0_cond_setup()
    _L0_cond_in = {k: v for k, v in _L0_cond_all.items() if k in ('W1', 'b1', 'W2', 'b2', 'We', 'be')}
    del _L0_cond_all
    return {'x': x, 'itok_B_0_7': itok_B_0_7, 'L0_cond_W1': _L0_cond_in['W1'], 'L0_cond_b1': _L0_cond_in['b1'], 'L0_cond_W2': _L0_cond_in['W2'], 'L0_cond_b2': _L0_cond_in['b2'], 'L0_cond_We': _L0_cond_in['We'], 'L0_cond_be': _L0_cond_in['be']}

def reference(x, itok_B_0_7, L0_cond_W1, L0_cond_b1, L0_cond_W2, L0_cond_b2, L0_cond_We, L0_cond_be):
    import jax
    import jax.numpy as jnp

    def _L0_cond_ref(x, indices, W1, b1, W2, b2, We, be):
        import jax, jax.numpy as jnp
        import numpy as np
        IN, HID, OUT, PART, E = (512, 2048, 512, 128, 8)
        B, N = (16, 1024)
        h = jax.nn.gelu(jnp.einsum('bni,ih->bnh', x, W1) + b1, approximate=False)
        shared_x = jnp.einsum('bnh,ho->bno', h, W2) + b2
        We_sel = We[indices]
        be_sel = be[indices]
        expert_x = jnp.einsum('bnh,bhp->bnp', h, We_sel) + be_sel[:, None, :]
        return jnp.concatenate([shared_x, expert_x], axis=-1)
    x = x + _L0_cond_ref(x, itok_B_0_7, L0_cond_W1, L0_cond_b1, L0_cond_W2, L0_cond_b2, L0_cond_We, L0_cond_be)
    return x

_drawn_inputs = setup_inputs


def setup_inputs(seed=0):
    import zlib

    import numpy as np

    out = dict(_drawn_inputs(seed))
    spreads = {}
    factors = {'L0_cond_b1': 6.363, 'L0_cond_b2': 4.872, 'L0_cond_be': 8.0}
    for name, (base, spread) in spreads.items():
        noise = np.random.default_rng([zlib.crc32(name.encode()), seed]).standard_normal(out[name].shape)
        drawn = base * np.exp(spread * noise) if base else spread * noise
        out[name] = jnp.asarray(drawn.astype(out[name].dtype))
    for name, factor in factors.items():
        out[name] = (out[name] * factor).astype(out[name].dtype)
    return out
```

```python
from contextlib import ExitStack

import concourse.bass as bass
from concourse import mybir


P = 128
B, N, IN, HID, OUT = 16, 512, 512, 2048, 512
PART, E = 128, 8
SHARED = OUT - PART
KC = IN // P
HT = HID // P
OT = OUT // P
ST = SHARED // P
WCOLS = IN + SHARED
W_RING = 4
H_BANKS = 4
HF_RING = 2
H_RING = 3
LAG = 2
EG = 4
GT = HT // EG
EARLY_W = W_RING + LAG + GT

F32 = mybir.dt.float32
F32R = mybir.dt.float32r
I32 = mybir.dt.int32
ALU = mybir.AluOpType
ACT = mybir.ActivationFunctionType


def build(nc, x, idx, w, we, b1, b2, be, out):
    with ExitStack() as ctx:
        def sb(name, shape, dt):
            return ctx.enter_context(nc.sbuf_tensor(name, shape, dt))

        def sem(name):
            return ctx.enter_context(nc.semaphore(name))

        w_hi = sb("w_hi", [P, HT, WCOLS], F32R)
        w_lo = sb("w_lo", [P, HT, WCOLS], F32R)
        e_hi = sb("e_hi", [P, EG, GT * PART], F32R)
        e_lo = sb("e_lo", [P, EG, GT * PART], F32R)
        w_raw = sb("w_raw", [P, W_RING, WCOLS], F32)
        e_raw = sb("e_raw", [P, EG, GT * PART], F32)
        x_raw = sb("x_raw", [P, 2, KC, N], F32)
        x_hi = sb("x_hi", [P, KC, N], F32R)
        x_lo = sb("x_lo", [P, KC, N], F32R)
        h_f32 = sb("h_f32", [P, HF_RING, N], F32)
        h_hi = sb("h_hi", [P, H_RING, N], F32R)
        h_lo = sb("h_lo", [P, H_RING, N], F32R)
        out_sb = sb("out_sb", [P, OT, N], F32)
        b1_sb = sb("b1_sb", [P, HT], F32)
        b2_sb = sb("b2_sb", [P, ST], F32)
        be_sb = sb("be_sb", [P, 2], F32)
        h_ps = ctx.enter_context(nc.psum_tensor("h_ps", [P, H_BANKS, N], F32))
        out_ps = ctx.enter_context(nc.psum_tensor("out_ps", [P, OT, N], F32))

        first_x_loaded = [sem(f"first_x_loaded{k}") for k in range(KC)]
        x_loaded = [sem("x_loaded_even"), sem("x_loaded_odd")]
        w_loaded = [sem(f"w_loaded{r}") for r in range(W_RING)]
        e_loaded = sem("e_loaded")
        biases_loaded = sem("biases_loaded")
        out_stored = [sem(f"out_stored{o}") for o in range(OT)]
        x_hi_done = sem("x_hi_done")
        x_lo_done = sem("x_lo_done")
        w_hi_done = sem("w_hi_done")
        w_lo_done = sem("w_lo_done")
        e_hi_done = sem("e_hi_done")
        e_lo_done = sem("e_lo_done")
        h_hi_done = sem("h_hi_done")
        h_lo_done = sem("h_lo_done")
        layer1_done = sem("layer1_done")
        layer2_done = sem("layer2_done")
        out_summed = sem("out_summed")
        out_ready = sem("out_ready")

        block = ctx.enter_context(nc.Block())

        def x_full(b, par):
            return 8 * b + 8 * par

        @block.sync
        def _(sp):
            def load_w(m):
                if m >= W_RING:
                    sp.wait_ge(w_lo_done, m - W_RING + 1)
                sp.dma_start(w_raw[:, m % W_RING, :], w[m]).then_inc(w_loaded[m % W_RING], 16)

            def load_x(b, par):
                sp.dma_start(x_raw[:, par], x[bass.ds(b, 1)].rearrange("a p k n -> (a p) k n")).then_inc(x_loaded[par], 16)

            def expert_of(b):
                return sp.value_load(idx[0:1, bass.ds(b, 1)], min_val=0, max_val=E - 1)

            def load_expert(e, par):
                sp.dma_start(e_raw[:, :, :],
                             we[bass.ds(e, 1)].rearrange("a p (g n) -> (a p) g n", g=EG)).then_inc(e_loaded, 16)
                sp.dma_start(be_sb[:, par:par + 1],
                             be[bass.ds(e, 1)].rearrange("a p n -> (a p) n")).then_inc(e_loaded, 16)

            def store(b):
                for o in range(OT):
                    sp.wait_ge(out_ready, OT * b + o + 1)
                    sp.dma_start(out[bass.ds(b, 1), o].rearrange("a p n -> (a p) n"),
                                 out_sb[:, o, :]).then_inc(out_stored[o], 16)

            sp.dma_start(x_raw[:, 0, 0], x[0, :, 0]).then_inc(first_x_loaded[0], 16)
            load_w(0)
            for k in range(1, KC):
                sp.dma_start(x_raw[:, 0, k], x[0, :, k]).then_inc(first_x_loaded[k], 16)
            sp.dma_start(b1_sb[:, :], b1).then_inc(biases_loaded, 16)
            load_w(1)
            load_expert(expert_of(0), 0)
            for m in range(2, W_RING):
                load_w(m)
            sp.dma_start(b2_sb[:, :], b2).then_inc(biases_loaded, 16)
            for m in range(W_RING, EARLY_W):
                load_w(m)
            e = expert_of(1)
            sp.wait_ge(e_lo_done, EG)
            load_expert(e, 1)
            for m in range(EARLY_W, HT):
                load_w(m)
            load_x(1, 1)
            store(0)
            with sp.Fori(0, B // 2 - 1) as pair:
                for par in (1, 0):
                    b = 2 * pair + 2 - par
                    sp.wait_ge(out_ready, OT * b)
                    load_x(b + 1, 1 - par)
                    e = expert_of(b + 1)
                    sp.wait_ge(e_lo_done, EG * b + EG)
                    load_expert(e, 1 - par)
                    store(b)
            store(B - 1)
            for o in range(OT):
                sp.wait_ge(out_stored[o], 16 * B)

        @block.scalar
        def _(act):
            def x_split(b, par, k):
                if isinstance(b, int) and b == 0:
                    act.wait_ge(first_x_loaded[k], 16)
                elif k == 0:
                    act.wait_ge(x_loaded[par], x_full(b, par))
                    act.wait_ge(layer1_done, HT * b)
                nc.scalar.activation(x_hi[:, k], x_raw[:, par, k], ACT.Copy).then_inc(x_hi_done, 1)

            def w_split(m):
                act.wait_ge(w_loaded[m % W_RING], 16 * (m // W_RING + 1))
                nc.scalar.activation(w_hi[:, m], w_raw[:, m % W_RING], ACT.Copy).then_inc(w_hi_done, 1)

            def e_split(b, g, first=False):
                act.wait_ge(e_loaded, 32 * b + 32)
                if not first:
                    if g < EG - 1:
                        act.wait_ge(layer2_done, (HT - 1) * (b - 1) + GT * (g + 1))
                    else:
                        act.wait_ge(out_summed, OT * b)
                nc.scalar.activation(e_hi[:, g], e_raw[:, g], ACT.Copy).then_inc(e_hi_done, 1)

            def gelu(b, m):
                act.wait_ge(layer1_done, HT * b + m + 1)
                if m >= HF_RING:
                    act.wait_ge(h_lo_done, HT * b + m - HF_RING + 1)
                if m >= H_RING:
                    act.wait_ge(layer2_done, (HT - 1) * b + m - H_RING + 1)
                bank, bias = h_ps[:, m % H_BANKS], b1_sb[:, m:m + 1]
                nc.scalar.activation(h_f32[:, m % HF_RING], bank, ACT.Gelu, bias=bias)
                nc.scalar.activation(h_hi[:, m % H_RING], bank, ACT.Gelu, bias=bias).then_inc(h_hi_done, 1)

            def batch(b, par, first=False, last=False):
                for m in range(HT):
                    gelu(b, m)
                    if first and m + LAG + 1 < HT:
                        w_split(m + LAG + 1)
                    if first and m in (1, 2):
                        e_split(b, m, first=True)
                    if m == 3:
                        e_split(b, EG - 1, first=first)
                    if m > 3 and m % GT == 3 and not last:
                        e_split(b + 1, m // GT - 1)
                if not last:
                    for k in range(KC):
                        x_split(b + 1, 1 - par, k)

            x_split(0, 0, 0)
            w_split(0)
            for k in range(1, KC):
                x_split(0, 0, k)
            w_split(1)
            e_split(0, 0, first=True)
            w_split(2)
            act.wait_ge(biases_loaded, 32)
            batch(0, 0, first=True)
            with act.Fori(0, B // 2 - 1) as pair:
                batch(2 * pair + 1, 1)
                batch(2 * pair + 2, 0)
            batch(B - 1, 1, last=True)

        @block.vector
        def _(dve):
            def x_split(b, par, k):
                dve.wait_ge(x_hi_done, KC * b + k + 1)
                nc.vector.tensor_tensor(x_lo[:, k], x_raw[:, par, k], x_hi[:, k].bitcast(F32),
                                        ALU.subtract).then_inc(x_lo_done, 1)

            def w_split(m):
                dve.wait_ge(w_hi_done, m + 1)
                nc.vector.tensor_tensor(w_lo[:, m], w_raw[:, m % W_RING], w_hi[:, m].bitcast(F32),
                                        ALU.subtract).then_inc(w_lo_done, 1)

            def e_split(b, g):
                dve.wait_ge(e_hi_done, EG * b + g + 1)
                nc.vector.tensor_tensor(e_lo[:, g], e_raw[:, g], e_hi[:, g].bitcast(F32),
                                        ALU.subtract).then_inc(e_lo_done, 1)

            def h_split(b, m):
                dve.wait_ge(h_hi_done, HT * b + m + 1)
                nc.vector.tensor_tensor(h_lo[:, m % H_RING], h_f32[:, m % HF_RING],
                                        h_hi[:, m % H_RING].bitcast(F32), ALU.subtract).then_inc(h_lo_done, 1)

            def finish(b, par, first=False):
                for o in range(OT):
                    dve.wait_ge(out_summed, OT * b + o + 1)
                    if not first:
                        dve.wait_ge(out_stored[o], 16 * b)
                    bias = b2_sb[:, o:o + 1] if o < ST else be_sb[:, par:par + 1]
                    nc.vector.scalar_tensor_tensor(out_sb[:, o], out_ps[:, o], bias, x_raw[:, par, o],
                                                   ALU.add, ALU.add).then_inc(out_ready, 1)

            def batch(b, par, first=False, last=False):
                for m in range(HT):
                    h_split(b, m)
                    if first and m + LAG + 1 < HT:
                        w_split(m + LAG + 1)
                    if first and m in (1, 2):
                        e_split(b, m)
                    if m == 3:
                        e_split(b, EG - 1)
                    if m > 3 and m % GT == 3 and not last:
                        e_split(b + 1, m // GT - 1)
                if not last:
                    for k in range(KC):
                        x_split(b + 1, 1 - par, k)
                finish(b, par, first)

            x_split(0, 0, 0)
            w_split(0)
            for k in range(1, KC):
                x_split(0, 0, k)
            w_split(1)
            e_split(0, 0)
            w_split(2)
            dve.wait_ge(biases_loaded, 32)
            batch(0, 0, first=True)
            with dve.Fori(0, B // 2 - 1) as pair:
                batch(2 * pair + 1, 1)
                batch(2 * pair + 2, 0)
            batch(B - 1, 1, last=True)

        @block.tensor
        def _(pe):
            def product(ps, hi, lo, v_hi, v_lo, start, stop):
                nc.tensor.matmul(ps, hi, v_hi, start=start, stop=False)
                nc.tensor.matmul(ps, hi, v_lo, start=False, stop=False)
                return nc.tensor.matmul(ps, lo, v_hi, start=False, stop=stop)

            def layer1(b, m, first):
                if first:
                    pe.wait_ge(w_lo_done, m + 1)
                if m >= H_BANKS:
                    pe.wait_ge(h_hi_done, HT * b + m - H_BANKS + 1)
                for k in range(KC):
                    if m == 0:
                        pe.wait_ge(x_lo_done, KC * b + k + 1)
                    c = slice(k * P, (k + 1) * P)
                    last = product(h_ps[:, m % H_BANKS], w_hi[:, m, c], w_lo[:, m, c],
                                   x_hi[:, k], x_lo[:, k], k == 0, k == KC - 1)
                last.then_inc(layer1_done, 1)

            def layer2(m, o):
                if o < ST:
                    hi, lo, c = w_hi[:, m], w_lo[:, m], slice(IN + o * P, IN + (o + 1) * P)
                else:
                    hi, lo, c = e_hi[:, m // GT], e_lo[:, m // GT], slice(m % GT * PART, (m % GT + 1) * PART)
                return product(out_ps[:, o], hi[:, c], lo[:, c], h_hi[:, m % H_RING], h_lo[:, m % H_RING],
                               m == 0, m == HT - 1)

            def layer2_inputs(b, m):
                pe.wait_ge(h_lo_done, HT * b + m + 1)
                if m % GT == 0:
                    pe.wait_ge(e_lo_done, EG * b + m // GT + 1)

            def batch(b, first=False):
                for m in range(HT):
                    layer1(b, m, first)
                    if m < LAG:
                        continue
                    layer2_inputs(b, m - LAG)
                    for o in range(OT):
                        if m == LAG and not first:
                            pe.wait_ge(out_ready, OT * (b - 1) + o + 1)
                        last = layer2(m - LAG, o)
                    last.then_inc(layer2_done, 1)
                layer2_inputs(b, HT - 2)
                for o in range(OT):
                    last = layer2(HT - 2, o)
                    if o == OT - 1:
                        last.then_inc(layer2_done, 1)
                    if o == 0:
                        layer2_inputs(b, HT - 1)
                    layer2(HT - 1, o).then_inc(out_summed, 1)

            batch(0, first=True)
            with pe.Fori(1, B) as b:
                batch(b)


def kernel(x, itok_B_0_7, L0_cond_W1, L0_cond_b1, L0_cond_W2, L0_cond_b2, L0_cond_We, L0_cond_be):
    import numpy as np
    import concourse.bacc as bacc
    from concourse.bass_utils import run_bass_kernel_spmd

    def rows(a, n):
        return np.asarray(a).reshape(n, P, -1)

    w1 = rows(L0_cond_W1, KC).reshape(KC, P, HT, P).transpose(2, 1, 0, 3).reshape(HT, P, IN)
    w2 = rows(L0_cond_W2, HT)
    arrays = {
        "x": np.asarray(x).reshape(B, N, KC, P).transpose(0, 3, 2, 1),
        "idx": np.asarray(itok_B_0_7).reshape(1, B),
        "w": np.concatenate([w1, w2], axis=2),
        "we": np.asarray(L0_cond_We).reshape(E, HT, P, PART).transpose(0, 2, 1, 3).reshape(E, P, HID),
        "b1": np.asarray(L0_cond_b1).reshape(HT, P).T,
        "b2": np.asarray(L0_cond_b2).reshape(ST, P).T,
        "be": np.asarray(L0_cond_be).reshape(E, P, 1),
    }
    arrays = {f"{k}_dram": np.ascontiguousarray(a) for k, a in arrays.items()}
    nc = bacc.Bacc("TRN2", target_bir_lowering=False, num_devices=1)
    args = [nc.dram_tensor(k, a.shape, mybir.dt.from_np(a.dtype), kind="ExternalInput").ap()
            for k, a in arrays.items()]
    out = nc.dram_tensor("out_dram", (B, OT, P, N), F32, kind="ExternalOutput").ap()
    build(nc, *args, out)
    got = run_bass_kernel_spmd(nc, [arrays], core_ids=[0]).results[0]["out_dram"]
    return got.transpose(0, 3, 1, 2).reshape(B, N, OUT)
```

```python
from contextlib import ExitStack

import concourse.bass as bass
from concourse import mybir


P = 128
B, N, IN, HID, OUT = 16, 512, 512, 2048, 512
PART, E = 128, 8
SHARED = OUT - PART
KC = IN // P
HT = HID // P
OT = OUT // P
ST = SHARED // P
WCOLS = IN + SHARED
W_RING = 4
H_BANKS = 4
HF_RING = 2
H_RING = 3
LAG = 2
WARM = 10
EG = 4
GT = HT // EG
EARLY_W = W_RING + LAG + GT

F32 = mybir.dt.float32
F32R = mybir.dt.float32r
BF16 = mybir.dt.bfloat16
ALU = mybir.AluOpType
ACT = mybir.ActivationFunctionType


def w_count(m, c=slice(0, WCOLS)):
    if m == 0:
        return 1 if c.stop == IN else 3
    return 2 if m == 1 else m + 2


def build(nc, x, idx, w, we, b1, b2, be, out):
    with ExitStack() as ctx:
        def sb(name, shape, dt):
            return ctx.enter_context(nc.sbuf_tensor(name, shape, dt))

        def sem(name):
            return ctx.enter_context(nc.semaphore(name))

        w_hi = sb("w_hi", [P, HT, WCOLS], F32R)
        w_lo = sb("w_lo", [P, HT, WCOLS], F32R)
        e_hi = sb("e_hi", [P, EG, GT * PART], F32R)
        e_lo = sb("e_lo", [P, EG, GT * PART], F32R)
        w_raw = sb("w_raw", [P, W_RING, WCOLS], F32)
        e_raw = sb("e_raw", [P, EG, GT * PART], F32)
        x_raw = sb("x_raw", [P, 2, KC, N], F32)
        x_hi = sb("x_hi", [P, KC, N], F32R)
        x_lo = sb("x_lo", [P, KC, N], F32R)
        h_f32 = sb("h_f32", [P, HF_RING, N], F32)
        h_hi = sb("h_hi", [P, H_RING, N], F32R)
        h_lo = sb("h_lo", [P, H_RING, N], F32R)
        out_sb = sb("out_sb", [P, OT, N], F32)
        b1_sb = sb("b1_sb", [P, HT], F32)
        b2_sb = sb("b2_sb", [P, ST], F32)
        be_sb = sb("be_sb", [P, 2], F32)
        warm = sb("warm", [P, N], BF16)
        gelu_warm = sb("gelu_warm", [P, 1], F32)
        h_ps = ctx.enter_context(nc.psum_tensor("h_ps", [P, H_BANKS, N], F32))
        out_ps = ctx.enter_context(nc.psum_tensor("out_ps", [P, OT, N], F32))

        first_x_loaded = [sem(f"first_x_loaded{k}") for k in range(KC)]
        x_loaded = [sem("x_loaded_even"), sem("x_loaded_odd")]
        w_loaded = [sem(f"w_loaded{r}") for r in range(W_RING)]
        first_w2_loaded = sem("first_w2_loaded")
        first_e_loaded = sem("first_e_loaded")
        e_loaded = sem("e_loaded")
        biases_loaded = sem("biases_loaded")
        out_stored = [sem(f"out_stored{o}") for o in range(OT)]
        warm_zeroed = sem("warm_zeroed")
        x_hi_done = sem("x_hi_done")
        x_lo_done = sem("x_lo_done")
        w_hi_done = sem("w_hi_done")
        w_lo_done = sem("w_lo_done")
        e_hi_done = sem("e_hi_done")
        e_lo_done = sem("e_lo_done")
        h_hi_done = sem("h_hi_done")
        h_lo_done = sem("h_lo_done")
        layer1_done = sem("layer1_done")
        layer2_done = sem("layer2_done")
        out_summed = sem("out_summed")
        out_ready = sem("out_ready")

        block = ctx.enter_context(nc.Block())

        def x_full(b, par):
            return 8 * b + 8 * par

        @block.sync
        def _(sp):
            def load_w(m):
                if m >= W_RING:
                    sp.wait_ge(w_lo_done, w_count(m - W_RING))
                sp.dma_start(w_raw[:, m % W_RING, :], w[m]).then_inc(w_loaded[m % W_RING], 16)

            def load_x(b, par):
                sp.dma_start(x_raw[:, par], x[bass.ds(b, 1)].rearrange("a p k n -> (a p) k n")).then_inc(x_loaded[par], 16)

            def expert_of(b):
                return sp.value_load(idx[0:1, bass.ds(b, 1)], min_val=0, max_val=E - 1)

            def load_expert(e, par, g0=0):
                groups = we[bass.ds(e, 1)].rearrange("a p (g n) -> (a p) g n", g=EG)
                sp.dma_start(e_raw[:, g0:], groups[:, g0:]).then_inc(e_loaded, 16)
                sp.dma_start(be_sb[:, par:par + 1],
                             be[bass.ds(e, 1)].rearrange("a p n -> (a p) n")).then_inc(e_loaded, 16)

            def store(b):
                for o in range(OT):
                    sp.wait_ge(out_ready, OT * b + o + 1)
                    sp.dma_start(out[bass.ds(b, 1), o].rearrange("a p n -> (a p) n"),
                                 out_sb[:, o, :]).then_inc(out_stored[o], 16)

            sp.dma_start(x_raw[:, 0, 0], x[0, :, 0]).then_inc(first_x_loaded[0], 16)
            sp.dma_start(w_raw[:, 0, :IN], w[0, :, :IN]).then_inc(w_loaded[0], 16)
            for k in range(1, KC):
                sp.dma_start(x_raw[:, 0, k], x[0, :, k]).then_inc(first_x_loaded[k], 16)
            sp.dma_start(b1_sb[:, :], b1).then_inc(biases_loaded, 16)
            load_w(1)
            sp.dma_start(w_raw[:, 0, IN:], w[0, :, IN:]).then_inc(first_w2_loaded, 16)
            load_w(2)
            e = expert_of(0)
            sp.dma_start(e_raw[:, 0], we[bass.ds(e, 1), :, :GT * PART].rearrange("a p n -> (a p) n")
                         ).then_inc(first_e_loaded, 16)
            load_w(W_RING - 1)
            load_expert(e, 0, 1)
            sp.dma_start(b2_sb[:, :], b2).then_inc(biases_loaded, 16)
            for m in range(W_RING, EARLY_W):
                load_w(m)
            e = expert_of(1)
            sp.wait_ge(e_lo_done, EG)
            load_expert(e, 1)
            for m in range(EARLY_W, HT):
                load_w(m)
            load_x(1, 1)
            store(0)
            with sp.Fori(0, B // 2 - 1) as pair:
                for par in (1, 0):
                    b = 2 * pair + 2 - par
                    sp.wait_ge(out_ready, OT * b)
                    load_x(b + 1, 1 - par)
                    e = expert_of(b + 1)
                    sp.wait_ge(e_lo_done, EG * b + EG)
                    load_expert(e, 1 - par)
                    store(b)
            store(B - 1)
            for o in range(OT):
                sp.wait_ge(out_stored[o], 16 * B)

        @block.scalar
        def _(act):
            def x_split(b, par, k):
                if isinstance(b, int) and b == 0:
                    act.wait_ge(first_x_loaded[k], 16)
                elif k == 0:
                    act.wait_ge(x_loaded[par], x_full(b, par))
                    act.wait_ge(layer1_done, HT * b)
                nc.scalar.activation(x_hi[:, k], x_raw[:, par, k], ACT.Copy).then_inc(x_hi_done, 1)

            def w_split(m, c=slice(0, WCOLS)):
                if c.start:
                    act.wait_ge(first_w2_loaded, 16)
                else:
                    act.wait_ge(w_loaded[m % W_RING], 16 * (m // W_RING + 1))
                nc.scalar.activation(w_hi[:, m, c], w_raw[:, m % W_RING, c], ACT.Copy).then_inc(w_hi_done, 1)

            def e_split(b, g, first=False):
                if first and g == 0:
                    act.wait_ge(first_e_loaded, 16)
                else:
                    act.wait_ge(e_loaded, 32 * b + 32)
                if not first:
                    if g < EG - 1:
                        act.wait_ge(layer2_done, (HT - 1) * (b - 1) + GT * (g + 1))
                    else:
                        act.wait_ge(out_summed, OT * b)
                nc.scalar.activation(e_hi[:, g], e_raw[:, g], ACT.Copy).then_inc(e_hi_done, 1)

            def gelu(b, m):
                act.wait_ge(layer1_done, HT * b + m + 1)
                if m >= HF_RING:
                    act.wait_ge(h_lo_done, HT * b + m - HF_RING + 1)
                if m >= H_RING:
                    act.wait_ge(layer2_done, (HT - 1) * b + m - H_RING + 1)
                bank, bias = h_ps[:, m % H_BANKS], b1_sb[:, m:m + 1]
                nc.scalar.activation(h_f32[:, m % HF_RING], bank, ACT.Gelu, bias=bias)
                nc.scalar.activation(h_hi[:, m % H_RING], bank, ACT.Gelu, bias=bias).then_inc(h_hi_done, 1)

            def batch(b, par, first=False, last=False):
                for m in range(HT):
                    gelu(b, m)
                    if first and m + LAG + 1 < HT:
                        w_split(m + LAG + 1)
                    if first and m in (1, 2):
                        e_split(b, m, first=True)
                    if m == 3:
                        e_split(b, EG - 1, first=first)
                    if m > 3 and m % GT == 3 and not last:
                        e_split(b + 1, m // GT - 1)
                if not last:
                    for k in range(KC):
                        x_split(b + 1, 1 - par, k)

            act.wait_ge(warm_zeroed, 1)
            nc.scalar.activation(gelu_warm[:, :], warm[:, 0:1], ACT.Gelu)
            x_split(0, 0, 0)
            w_split(0, slice(0, IN))
            for k in range(1, KC):
                x_split(0, 0, k)
            w_split(1)
            w_split(0, slice(IN, WCOLS))
            w_split(2)
            e_split(0, 0, first=True)
            act.wait_ge(biases_loaded, 32)
            batch(0, 0, first=True)
            with act.Fori(0, B // 2 - 1) as pair:
                batch(2 * pair + 1, 1)
                batch(2 * pair + 2, 0)
            batch(B - 1, 1, last=True)

        @block.vector
        def _(dve):
            def x_split(b, par, k):
                dve.wait_ge(x_hi_done, KC * b + k + 1)
                nc.vector.tensor_tensor(x_lo[:, k], x_raw[:, par, k], x_hi[:, k].bitcast(F32),
                                        ALU.subtract).then_inc(x_lo_done, 1)

            def w_split(m, c=slice(0, WCOLS)):
                dve.wait_ge(w_hi_done, w_count(m, c))
                nc.vector.tensor_tensor(w_lo[:, m, c], w_raw[:, m % W_RING, c], w_hi[:, m, c].bitcast(F32),
                                        ALU.subtract).then_inc(w_lo_done, 1)

            def e_split(b, g):
                dve.wait_ge(e_hi_done, EG * b + g + 1)
                nc.vector.tensor_tensor(e_lo[:, g], e_raw[:, g], e_hi[:, g].bitcast(F32),
                                        ALU.subtract).then_inc(e_lo_done, 1)

            def h_split(b, m):
                dve.wait_ge(h_hi_done, HT * b + m + 1)
                nc.vector.tensor_tensor(h_lo[:, m % H_RING], h_f32[:, m % HF_RING],
                                        h_hi[:, m % H_RING].bitcast(F32), ALU.subtract).then_inc(h_lo_done, 1)

            def finish(b, par, first=False):
                for o in range(OT):
                    dve.wait_ge(out_summed, OT * b + o + 1)
                    if not first:
                        dve.wait_ge(out_stored[o], 16 * b)
                    bias = b2_sb[:, o:o + 1] if o < ST else be_sb[:, par:par + 1]
                    nc.vector.scalar_tensor_tensor(out_sb[:, o], out_ps[:, o], bias, x_raw[:, par, o],
                                                   ALU.add, ALU.add).then_inc(out_ready, 1)

            def batch(b, par, first=False, last=False):
                for m in range(HT):
                    h_split(b, m)
                    if first and m + LAG + 1 < HT:
                        w_split(m + LAG + 1)
                    if first and m in (1, 2):
                        e_split(b, m)
                    if m == 3:
                        e_split(b, EG - 1)
                    if m > 3 and m % GT == 3 and not last:
                        e_split(b + 1, m // GT - 1)
                if not last:
                    for k in range(KC):
                        x_split(b + 1, 1 - par, k)
                finish(b, par, first)

            nc.vector.memset(warm[:, :], 0.0).then_inc(warm_zeroed, 1)
            x_split(0, 0, 0)
            w_split(0, slice(0, IN))
            for k in range(1, KC):
                x_split(0, 0, k)
            w_split(1)
            w_split(0, slice(IN, WCOLS))
            w_split(2)
            e_split(0, 0)
            dve.wait_ge(biases_loaded, 32)
            batch(0, 0, first=True)
            with dve.Fori(0, B // 2 - 1) as pair:
                batch(2 * pair + 1, 1)
                batch(2 * pair + 2, 0)
            batch(B - 1, 1, last=True)

        @block.tensor
        def _(pe):
            def product(ps, hi, lo, v_hi, v_lo, start, stop):
                nc.tensor.matmul(ps, hi, v_hi, start=start, stop=False)
                nc.tensor.matmul(ps, hi, v_lo, start=False, stop=False)
                return nc.tensor.matmul(ps, lo, v_hi, start=False, stop=stop)

            def layer1(b, m, first):
                if first:
                    pe.wait_ge(w_lo_done, w_count(m, slice(0, IN)) if m == 0 else w_count(m))
                if m >= H_BANKS:
                    pe.wait_ge(h_hi_done, HT * b + m - H_BANKS + 1)
                for k in range(KC):
                    if m == 0:
                        pe.wait_ge(x_lo_done, KC * b + k + 1)
                    c = slice(k * P, (k + 1) * P)
                    last = product(h_ps[:, m % H_BANKS], w_hi[:, m, c], w_lo[:, m, c],
                                   x_hi[:, k], x_lo[:, k], k == 0, k == KC - 1)
                last.then_inc(layer1_done, 1)

            def layer2(m, o):
                if o < ST:
                    hi, lo, c = w_hi[:, m], w_lo[:, m], slice(IN + o * P, IN + (o + 1) * P)
                else:
                    hi, lo, c = e_hi[:, m // GT], e_lo[:, m // GT], slice(m % GT * PART, (m % GT + 1) * PART)
                return product(out_ps[:, o], hi[:, c], lo[:, c], h_hi[:, m % H_RING], h_lo[:, m % H_RING],
                               m == 0, m == HT - 1)

            def layer2_inputs(b, m):
                pe.wait_ge(h_lo_done, HT * b + m + 1)
                if m % GT == 0:
                    pe.wait_ge(e_lo_done, EG * b + m // GT + 1)

            def batch(b, first=False):
                for m in range(HT):
                    layer1(b, m, first)
                    if m < LAG:
                        continue
                    layer2_inputs(b, m - LAG)
                    for o in range(OT):
                        if m == LAG and not first:
                            pe.wait_ge(out_ready, OT * (b - 1) + o + 1)
                        last = layer2(m - LAG, o)
                    last.then_inc(layer2_done, 1)
                layer2_inputs(b, HT - 2)
                for o in range(OT + LAG):
                    if o < OT:
                        last = layer2(HT - 2, o)
                        if o == OT - 1:
                            last.then_inc(layer2_done, 1)
                    if o == LAG:
                        layer2_inputs(b, HT - 1)
                    if o >= LAG:
                        layer2(HT - 1, o - LAG).then_inc(out_summed, 1)

            pe.wait_ge(warm_zeroed, 1)
            for _ in range(WARM):
                nc.tensor.matmul(h_ps[:, H_BANKS - 1], warm[:, :P], warm[:, :], start=True, stop=True)
            batch(0, first=True)
            with pe.Fori(1, B) as b:
                batch(b)


def kernel(x, itok_B_0_7, L0_cond_W1, L0_cond_b1, L0_cond_W2, L0_cond_b2, L0_cond_We, L0_cond_be):
    import numpy as np
    import concourse.bacc as bacc
    from concourse.bass_utils import run_bass_kernel_spmd

    def rows(a, n):
        return np.asarray(a).reshape(n, P, -1)

    w1 = rows(L0_cond_W1, KC).reshape(KC, P, HT, P).transpose(2, 1, 0, 3).reshape(HT, P, IN)
    w2 = rows(L0_cond_W2, HT)
    arrays = {
        "x": np.asarray(x).reshape(B, N, KC, P).transpose(0, 3, 2, 1),
        "idx": np.asarray(itok_B_0_7).reshape(1, B),
        "w": np.concatenate([w1, w2], axis=2),
        "we": np.asarray(L0_cond_We).reshape(E, HT, P, PART).transpose(0, 2, 1, 3).reshape(E, P, HID),
        "b1": np.asarray(L0_cond_b1).reshape(HT, P).T,
        "b2": np.asarray(L0_cond_b2).reshape(ST, P).T,
        "be": np.asarray(L0_cond_be).reshape(E, P, 1),
    }
    arrays = {f"{k}_dram": np.ascontiguousarray(a) for k, a in arrays.items()}
    nc = bacc.Bacc("TRN2", target_bir_lowering=False, num_devices=1)
    args = [nc.dram_tensor(k, a.shape, mybir.dt.from_np(a.dtype), kind="ExternalInput").ap()
            for k, a in arrays.items()]
    out = nc.dram_tensor("out_dram", (B, OT, P, N), F32, kind="ExternalOutput").ap()
    build(nc, *args, out)
    got = run_bass_kernel_spmd(nc, [arrays], core_ids=[0]).results[0]["out_dram"]
    return got.transpose(0, 3, 1, 2).reshape(B, N, OUT)
```

```python
from contextlib import ExitStack

import concourse.bass as bass
from concourse import mybir


P = 128
B, N, IN, HID, OUT = 16, 512, 512, 2048, 512
PART, E = 128, 8
SHARED = OUT - PART
KC = IN // P
HT = HID // P
OT = OUT // P
ST = SHARED // P
WCOLS = IN + SHARED
W_RING = 4
H_BANKS = 4
HF_RING = 2
H_RING = 3
LAG = 2
WARM = 10
EG = 4
GT = HT // EG
EARLY_W = W_RING + LAG + GT

F32 = mybir.dt.float32
F32R = mybir.dt.float32r
BF16 = mybir.dt.bfloat16
ALU = mybir.AluOpType
ACT = mybir.ActivationFunctionType


LAYER1, LAYER2, WHOLE = slice(0, IN), slice(IN, WCOLS), slice(0, WCOLS)
PARTED = LAG + 1


def w_count(m, part=WHOLE):
    return m + 1 if part is LAYER1 else m + PARTED + 1


def build(nc, x, idx, w, we, b1, b2, be, out):
    with ExitStack() as ctx:
        def sb(name, shape, dt):
            return ctx.enter_context(nc.sbuf_tensor(name, shape, dt))

        def sem(name):
            return ctx.enter_context(nc.semaphore(name))

        w_hi = sb("w_hi", [P, HT, WCOLS], F32R)
        w_lo = sb("w_lo", [P, HT, WCOLS], F32R)
        e_hi = sb("e_hi", [P, EG, GT * PART], F32R)
        e_lo = sb("e_lo", [P, EG, GT * PART], F32R)
        w_raw = sb("w_raw", [P, W_RING, WCOLS], F32)
        e_raw = sb("e_raw", [P, EG, GT * PART], F32)
        x_raw = sb("x_raw", [P, 2, KC, N], F32)
        x_hi = sb("x_hi", [P, KC, N], F32R)
        x_lo = sb("x_lo", [P, KC, N], F32R)
        h_f32 = sb("h_f32", [P, HF_RING, N], F32)
        h_hi = sb("h_hi", [P, H_RING, N], F32R)
        h_lo = sb("h_lo", [P, H_RING, N], F32R)
        out_sb = sb("out_sb", [P, OT, N], F32)
        b1_sb = sb("b1_sb", [P, HT], F32)
        b2_sb = sb("b2_sb", [P, ST], F32)
        be_sb = sb("be_sb", [P, 2], F32)
        warm = sb("warm", [P, N], BF16)
        gelu_warm = sb("gelu_warm", [P, 1], F32)
        h_ps = ctx.enter_context(nc.psum_tensor("h_ps", [P, H_BANKS, N], F32))
        out_ps = ctx.enter_context(nc.psum_tensor("out_ps", [P, OT, N], F32))

        first_x_loaded = [sem(f"first_x_loaded{k}") for k in range(KC)]
        x_loaded = [sem("x_loaded_even"), sem("x_loaded_odd")]
        w_loaded = [sem(f"w_loaded{r}") for r in range(W_RING)]
        first_w2_loaded = [sem(f"first_w2_loaded{m}") for m in range(PARTED)]
        first_e_loaded = sem("first_e_loaded")
        e_loaded = sem("e_loaded")
        biases_loaded = sem("biases_loaded")
        out_stored = [sem(f"out_stored{o}") for o in range(OT)]
        warm_zeroed = sem("warm_zeroed")
        x_hi_done = sem("x_hi_done")
        x_lo_done = sem("x_lo_done")
        w_hi_done = sem("w_hi_done")
        w_lo_done = sem("w_lo_done")
        e_hi_done = sem("e_hi_done")
        e_lo_done = sem("e_lo_done")
        h_hi_done = sem("h_hi_done")
        h_lo_done = sem("h_lo_done")
        layer1_done = sem("layer1_done")
        layer2_done = sem("layer2_done")
        out_summed = sem("out_summed")
        out_ready = sem("out_ready")

        block = ctx.enter_context(nc.Block())

        def x_full(b, par):
            return 8 * b + 8 * par

        @block.sync
        def _(sp):
            def load_part(m, part, loaded):
                sp.dma_start(w_raw[:, m, part], w[m, :, part]).then_inc(loaded[m], 16)

            def load_w(m):
                if m >= W_RING:
                    sp.wait_ge(w_lo_done, w_count(m - W_RING))
                sp.dma_start(w_raw[:, m % W_RING, :], w[m]).then_inc(w_loaded[m % W_RING], 16)

            def load_x(b, par):
                sp.dma_start(x_raw[:, par], x[bass.ds(b, 1)].rearrange("a p k n -> (a p) k n")).then_inc(x_loaded[par], 16)

            def expert_of(b):
                return sp.value_load(idx[0:1, bass.ds(b, 1)], min_val=0, max_val=E - 1)

            def load_expert(e, par, g0=0):
                groups = we[bass.ds(e, 1)].rearrange("a p (g n) -> (a p) g n", g=EG)
                sp.dma_start(e_raw[:, g0:], groups[:, g0:]).then_inc(e_loaded, 16)
                sp.dma_start(be_sb[:, par:par + 1],
                             be[bass.ds(e, 1)].rearrange("a p n -> (a p) n")).then_inc(e_loaded, 16)

            def store(b):
                for o in range(OT):
                    sp.wait_ge(out_ready, OT * b + o + 1)
                    sp.dma_start(out[bass.ds(b, 1), o].rearrange("a p n -> (a p) n"),
                                 out_sb[:, o, :]).then_inc(out_stored[o], 16)

            sp.dma_start(x_raw[:, 0, 0], x[0, :, 0]).then_inc(first_x_loaded[0], 16)
            load_part(0, LAYER1, w_loaded)
            for k in range(1, KC):
                sp.dma_start(x_raw[:, 0, k], x[0, :, k]).then_inc(first_x_loaded[k], 16)
            sp.dma_start(b1_sb[:, :], b1).then_inc(biases_loaded, 16)
            sp.dma_start(b2_sb[:, :], b2).then_inc(biases_loaded, 16)
            for m in range(1, PARTED):
                load_part(m, LAYER1, w_loaded)
            load_part(0, LAYER2, first_w2_loaded)
            e = expert_of(0)
            sp.dma_start(e_raw[:, 0], we[bass.ds(e, 1), :, :GT * PART].rearrange("a p n -> (a p) n")
                         ).then_inc(first_e_loaded, 16)
            for m in range(1, PARTED):
                load_part(m, LAYER2, first_w2_loaded)
            for m in range(PARTED, W_RING):
                load_w(m)
            load_expert(e, 0, 1)
            for m in range(W_RING, EARLY_W):
                load_w(m)
            e = expert_of(1)
            sp.wait_ge(e_lo_done, EG)
            load_expert(e, 1)
            for m in range(EARLY_W, HT):
                load_w(m)
            load_x(1, 1)
            store(0)
            with sp.Fori(0, B // 2 - 1) as pair:
                for par in (1, 0):
                    b = 2 * pair + 2 - par
                    sp.wait_ge(out_ready, OT * b)
                    load_x(b + 1, 1 - par)
                    e = expert_of(b + 1)
                    sp.wait_ge(e_lo_done, EG * b + EG)
                    load_expert(e, 1 - par)
                    store(b)
            store(B - 1)
            for o in range(OT):
                sp.wait_ge(out_stored[o], 16 * B)

        @block.scalar
        def _(act):
            def x_split(b, par, k):
                if isinstance(b, int) and b == 0:
                    act.wait_ge(first_x_loaded[k], 16)
                elif k == 0:
                    act.wait_ge(x_loaded[par], x_full(b, par))
                    act.wait_ge(layer1_done, HT * b)
                nc.scalar.activation(x_hi[:, k], x_raw[:, par, k], ACT.Copy).then_inc(x_hi_done, 1)

            def w_split(m, part=WHOLE):
                if part is LAYER2:
                    act.wait_ge(first_w2_loaded[m], 16)
                else:
                    act.wait_ge(w_loaded[m % W_RING], 16 * (m // W_RING + 1))
                nc.scalar.activation(w_hi[:, m, part], w_raw[:, m % W_RING, part], ACT.Copy).then_inc(w_hi_done, 1)

            def e_split(b, g, first=False):
                if first and g == 0:
                    act.wait_ge(first_e_loaded, 16)
                else:
                    act.wait_ge(e_loaded, 32 * b + 32)
                if not first:
                    if g < EG - 1:
                        act.wait_ge(layer2_done, (HT - 1) * (b - 1) + GT * (g + 1))
                    else:
                        act.wait_ge(out_summed, OT * b)
                nc.scalar.activation(e_hi[:, g], e_raw[:, g], ACT.Copy).then_inc(e_hi_done, 1)

            def gelu(b, m):
                act.wait_ge(layer1_done, HT * b + m + 1)
                if m >= HF_RING:
                    act.wait_ge(h_lo_done, HT * b + m - HF_RING + 1)
                if m >= H_RING:
                    act.wait_ge(layer2_done, (HT - 1) * b + m - H_RING + 1)
                bank, bias = h_ps[:, m % H_BANKS], b1_sb[:, m:m + 1]
                nc.scalar.activation(h_f32[:, m % HF_RING], bank, ACT.Gelu, bias=bias)
                nc.scalar.activation(h_hi[:, m % H_RING], bank, ACT.Gelu, bias=bias).then_inc(h_hi_done, 1)

            def batch(b, par, first=False, last=False):
                for m in range(HT):
                    gelu(b, m)
                    if first and m + PARTED < HT:
                        w_split(m + PARTED)
                    if first and m in (1, 2):
                        e_split(b, m, first=True)
                    if m == 3:
                        e_split(b, EG - 1, first=first)
                    if m > 3 and m % GT == 3 and not last:
                        e_split(b + 1, m // GT - 1)
                if not last:
                    for k in range(KC):
                        x_split(b + 1, 1 - par, k)

            act.wait_ge(warm_zeroed, 1)
            nc.scalar.activation(gelu_warm[:, :], warm[:, 0:1], ACT.Gelu)
            x_split(0, 0, 0)
            w_split(0, LAYER1)
            for k in range(1, KC):
                x_split(0, 0, k)
            for m in range(1, PARTED):
                w_split(m, LAYER1)
            w_split(0, LAYER2)
            e_split(0, 0, first=True)
            for m in range(1, PARTED):
                w_split(m, LAYER2)
            act.wait_ge(biases_loaded, 32)
            batch(0, 0, first=True)
            with act.Fori(0, B // 2 - 1) as pair:
                batch(2 * pair + 1, 1)
                batch(2 * pair + 2, 0)
            batch(B - 1, 1, last=True)

        @block.vector
        def _(dve):
            def x_split(b, par, k):
                dve.wait_ge(x_hi_done, KC * b + k + 1)
                nc.vector.tensor_tensor(x_lo[:, k], x_raw[:, par, k], x_hi[:, k].bitcast(F32),
                                        ALU.subtract).then_inc(x_lo_done, 1)

            def w_split(m, part=WHOLE):
                dve.wait_ge(w_hi_done, w_count(m, part))
                nc.vector.tensor_tensor(w_lo[:, m, part], w_raw[:, m % W_RING, part], w_hi[:, m, part].bitcast(F32),
                                        ALU.subtract).then_inc(w_lo_done, 1)

            def e_split(b, g):
                dve.wait_ge(e_hi_done, EG * b + g + 1)
                nc.vector.tensor_tensor(e_lo[:, g], e_raw[:, g], e_hi[:, g].bitcast(F32),
                                        ALU.subtract).then_inc(e_lo_done, 1)

            def h_split(b, m):
                dve.wait_ge(h_hi_done, HT * b + m + 1)
                nc.vector.tensor_tensor(h_lo[:, m % H_RING], h_f32[:, m % HF_RING],
                                        h_hi[:, m % H_RING].bitcast(F32), ALU.subtract).then_inc(h_lo_done, 1)

            def finish(b, par, first=False):
                for o in range(OT):
                    dve.wait_ge(out_summed, OT * b + o + 1)
                    if not first:
                        dve.wait_ge(out_stored[o], 16 * b)
                    bias = b2_sb[:, o:o + 1] if o < ST else be_sb[:, par:par + 1]
                    nc.vector.scalar_tensor_tensor(out_sb[:, o], out_ps[:, o], bias, x_raw[:, par, o],
                                                   ALU.add, ALU.add).then_inc(out_ready, 1)

            def batch(b, par, first=False, last=False):
                for m in range(HT):
                    h_split(b, m)
                    if first and m + PARTED < HT:
                        w_split(m + PARTED)
                    if first and m in (1, 2):
                        e_split(b, m)
                    if m == 3:
                        e_split(b, EG - 1)
                    if m > 3 and m % GT == 3 and not last:
                        e_split(b + 1, m // GT - 1)
                if not last:
                    for k in range(KC):
                        x_split(b + 1, 1 - par, k)
                finish(b, par, first)

            nc.vector.memset(warm[:, :], 0.0).then_inc(warm_zeroed, 1)
            x_split(0, 0, 0)
            w_split(0, LAYER1)
            for k in range(1, KC):
                x_split(0, 0, k)
            for m in range(1, PARTED):
                w_split(m, LAYER1)
            w_split(0, LAYER2)
            e_split(0, 0)
            for m in range(1, PARTED):
                w_split(m, LAYER2)
            dve.wait_ge(biases_loaded, 32)
            batch(0, 0, first=True)
            with dve.Fori(0, B // 2 - 1) as pair:
                batch(2 * pair + 1, 1)
                batch(2 * pair + 2, 0)
            batch(B - 1, 1, last=True)

        @block.tensor
        def _(pe):
            def product(ps, hi, lo, v_hi, v_lo, start, stop):
                nc.tensor.matmul(ps, hi, v_hi, start=start, stop=False)
                nc.tensor.matmul(ps, hi, v_lo, start=False, stop=False)
                return nc.tensor.matmul(ps, lo, v_hi, start=False, stop=stop)

            def layer1(b, m, first):
                if first:
                    pe.wait_ge(w_lo_done, w_count(m, LAYER1 if m < PARTED else WHOLE))
                if m >= H_BANKS:
                    pe.wait_ge(h_hi_done, HT * b + m - H_BANKS + 1)
                for k in range(KC):
                    if m == 0:
                        pe.wait_ge(x_lo_done, KC * b + k + 1)
                    c = slice(k * P, (k + 1) * P)
                    last = product(h_ps[:, m % H_BANKS], w_hi[:, m, c], w_lo[:, m, c],
                                   x_hi[:, k], x_lo[:, k], k == 0, k == KC - 1)
                last.then_inc(layer1_done, 1)

            def layer2(m, o):
                if o < ST:
                    hi, lo, c = w_hi[:, m], w_lo[:, m], slice(IN + o * P, IN + (o + 1) * P)
                else:
                    hi, lo, c = e_hi[:, m // GT], e_lo[:, m // GT], slice(m % GT * PART, (m % GT + 1) * PART)
                return product(out_ps[:, o], hi[:, c], lo[:, c], h_hi[:, m % H_RING], h_lo[:, m % H_RING],
                               m == 0, m == HT - 1)

            def layer2_inputs(b, m):
                pe.wait_ge(h_lo_done, HT * b + m + 1)
                if m % GT == 0:
                    pe.wait_ge(e_lo_done, EG * b + m // GT + 1)

            def batch(b, first=False):
                for m in range(HT):
                    layer1(b, m, first)
                    if m < LAG:
                        continue
                    if first and m == LAG:
                        pe.wait_ge(w_lo_done, w_count(0, LAYER2))
                    layer2_inputs(b, m - LAG)
                    for o in range(OT):
                        if m == LAG and not first:
                            pe.wait_ge(out_ready, OT * (b - 1) + o + 1)
                        last = layer2(m - LAG, o)
                    last.then_inc(layer2_done, 1)
                layer2_inputs(b, HT - 2)
                for o in range(OT + LAG):
                    if o < OT:
                        last = layer2(HT - 2, o)
                        if o == OT - 1:
                            last.then_inc(layer2_done, 1)
                    if o == LAG:
                        layer2_inputs(b, HT - 1)
                    if o >= LAG:
                        layer2(HT - 1, o - LAG).then_inc(out_summed, 1)

            pe.wait_ge(warm_zeroed, 1)
            for _ in range(WARM):
                nc.tensor.matmul(h_ps[:, H_BANKS - 1], warm[:, :P], warm[:, :], start=True, stop=True)
            batch(0, first=True)
            with pe.Fori(1, B) as b:
                batch(b)


def kernel(x, itok_B_0_7, L0_cond_W1, L0_cond_b1, L0_cond_W2, L0_cond_b2, L0_cond_We, L0_cond_be):
    import numpy as np
    import concourse.bacc as bacc
    from concourse.bass_utils import run_bass_kernel_spmd

    def rows(a, n):
        return np.asarray(a).reshape(n, P, -1)

    w1 = rows(L0_cond_W1, KC).reshape(KC, P, HT, P).transpose(2, 1, 0, 3).reshape(HT, P, IN)
    w2 = rows(L0_cond_W2, HT)
    arrays = {
        "x": np.asarray(x).reshape(B, N, KC, P).transpose(0, 3, 2, 1),
        "idx": np.asarray(itok_B_0_7).reshape(1, B),
        "w": np.concatenate([w1, w2], axis=2),
        "we": np.asarray(L0_cond_We).reshape(E, HT, P, PART).transpose(0, 2, 1, 3).reshape(E, P, HID),
        "b1": np.asarray(L0_cond_b1).reshape(HT, P).T,
        "b2": np.asarray(L0_cond_b2).reshape(ST, P).T,
        "be": np.asarray(L0_cond_be).reshape(E, P, 1),
    }
    arrays = {f"{k}_dram": np.ascontiguousarray(a) for k, a in arrays.items()}
    nc = bacc.Bacc("TRN2", target_bir_lowering=False, num_devices=1)
    args = [nc.dram_tensor(k, a.shape, mybir.dt.from_np(a.dtype), kind="ExternalInput").ap()
            for k, a in arrays.items()]
    out = nc.dram_tensor("out_dram", (B, OT, P, N), F32, kind="ExternalOutput").ap()
    build(nc, *args, out)
    got = run_bass_kernel_spmd(nc, [arrays], core_ids=[0]).results[0]["out_dram"]
    return got.transpose(0, 3, 1, 2).reshape(B, N, OUT)
```
